# Optimizing a Trainium2 kernel written in Bass

```python
import numpy as np
import jax
import jax.numpy as jnp

def _softmax(x, axis=-1):
    return jax.nn.softmax(x, axis=axis)

def _gelu(x):
    return jax.nn.gelu(x, approximate=True)

def _silu(x):
    return jax.nn.silu(x)

def _sigmoid(x):
    return jax.nn.sigmoid(x)

def _layernorm(x, axis=-1, eps=1e-05):
    m = jnp.mean(x, axis=axis, keepdims=True)
    v = jnp.var(x, axis=axis, keepdims=True)
    return (x - m) / jnp.sqrt(v + eps)

def _scatter_add(tgt, idx, src, axis=0):
    return tgt.at[idx].add(src)

def _segment_sum(src, seg, n):
    return jax.ops.segment_sum(src, seg, n)
kernel_name = 'mk_adj_resnorm_d1_adj_r2_bd756d'

def setup_inputs(seed: int=0):
    np.random.seed(seed)
    _w = jnp.asarray

    def _rec_inputs():
        import jax
        import jax.numpy as jnp
        _gk = jax.random.key(seed)
        x = -0.0001538 + 1 * jax.random.normal(jax.random.fold_in(_gk, 1), (64, 128, 384), jnp.float32)
        _a = jax.random.bernoulli(jax.random.fold_in(_gk, 2), 0.0625, (64, 128, 128))
        _a = jnp.logical_or(_a, jnp.swapaxes(_a, -1, -2))
        _a = jnp.logical_or(_a, jnp.eye(128, dtype=bool))
        _af = _a.astype(jnp.float32)
        _af = _af * jax.random.uniform(jax.random.fold_in(_gk, 3), (64, 128, 128), jnp.float32, 0.05, 0.999992)
        adj = _af
        return (x, adj)
    x, adj = _rec_inputs()

    def _L0_gnn_setup():
        import jax, jax.numpy as jnp
        import numpy as np
        B, N, D, H = (8, 512, 384, 12)
        HD = D // H

        def _split_heads(x):
            b, n, _ = x.shape
            return x.reshape(b, n, H, HD).transpose(0, 2, 1, 3)
        key = jax.random.key(seed)
        ks = jax.random.split(key, 10)
        input_graph = jax.random.normal(ks[0], (B, N, D), dtype=jnp.float32)
        u = jax.random.uniform(ks[1], (B, N, N), dtype=jnp.float32)
        keep = jax.random.uniform(ks[2], (B, N, N)) < 0.15
        adj = jnp.where(keep, u, 0.0)
        s = 1.0 / np.sqrt(D)
        Wq = jax.random.normal(ks[3], (D, D), dtype=jnp.float32) * s
        bq = jnp.zeros((D,), dtype=jnp.float32)
        Wk = jax.random.normal(ks[4], (D, D), dtype=jnp.float32) * s
        bk = jnp.zeros((D,), dtype=jnp.float32)
        Wv = jax.random.normal(ks[5], (D, D), dtype=jnp.float32) * s
        bv = jnp.zeros((D,), dtype=jnp.float32)
        beta = jnp.asarray(0.1, dtype=jnp.float32)
        return {'input_graph': input_graph, 'adj': adj, 'Wq': Wq, 'bq': bq, 'Wk': Wk, 'bk': bk, 'Wv': Wv, 'bv': bv, 'beta': beta}
    _L0_gnn_all = _L0_gnn_setup()
    _L0_gnn_in = {k: v for k, v in _L0_gnn_all.items() if k in ('Wq', 'bq', 'Wk', 'bk', 'Wv', 'bv', 'beta')}
    del _L0_gnn_all
    return {'x': x, 'adj': adj, 'L0_gnn_Wq': _L0_gnn_in['Wq'], 'L0_gnn_bq': _L0_gnn_in['bq'], 'L0_gnn_Wk': _L0_gnn_in['Wk'], 'L0_gnn_bk': _L0_gnn_in['bk'], 'L0_gnn_Wv': _L0_gnn_in['Wv'], 'L0_gnn_bv': _L0_gnn_in['bv'], 'L0_gnn_beta': _L0_gnn_in['beta']}

def reference(x, adj, L0_gnn_Wq, L0_gnn_bq, L0_gnn_Wk, L0_gnn_bk, L0_gnn_Wv, L0_gnn_bv, L0_gnn_beta):
    import jax
    import jax.numpy as jnp

    def _L0_gnn_ref(input_graph, adj, Wq, bq, Wk, bk, Wv, bv, beta):
        import jax, jax.numpy as jnp
        import numpy as np
        B, N, D, H = (8, 512, 384, 12)
        HD = D // H

        def _split_heads(x):
            b, n, _ = x.shape
            return x.reshape(b, n, H, HD).transpose(0, 2, 1, 3)
        q = _split_heads(input_graph @ Wq + bq)
        k = _split_heads(input_graph @ Wk + bk)
        v = _split_heads(input_graph @ Wv + bv)
        scores = jnp.einsum('bhqd,bhkd->bhqk', q, k) / jnp.sqrt(jnp.asarray(HD, input_graph.dtype))
        adj_e = adj[:, None, :, :]
        scores = scores + beta * adj_e
        scores = jnp.where(adj_e > 0, scores, jnp.asarray(-9000000000000000.0, scores.dtype))
        probs = jax.nn.softmax(scores, axis=-1)
        out = jnp.einsum('bhqk,bhkd->bhqd', probs, v)
        return out.transpose(0, 2, 1, 3).reshape(input_graph.shape[0], input_graph.shape[1], D)
    x = _layernorm(x + _L0_gnn_ref(x, adj, L0_gnn_Wq, L0_gnn_bq, L0_gnn_Wk, L0_gnn_bk, L0_gnn_Wv, L0_gnn_bv, L0_gnn_beta), axis=-1)
    return x

_drawn_inputs = setup_inputs


def setup_inputs(seed=0):
    import zlib

    import numpy as np

    out = dict(_drawn_inputs(seed))
    spreads = {'L0_gnn_bq': (0.0, 0.274), 'L0_gnn_bk': (0.0, 0.8), 'L0_gnn_bv': (0.0, 0.1)}
    factors = {}
    for name, (base, spread) in spreads.items():
        noise = np.random.default_rng([zlib.crc32(name.encode()), seed]).standard_normal(out[name].shape)
        drawn = base * np.exp(spread * noise) if base else spread * noise
        out[name] = jnp.asarray(drawn.astype(out[name].dtype))
    for name, factor in factors.items():
        out[name] = (out[name] * factor).astype(out[name].dtype)
    return out
```

```python
from contextlib import ExitStack

import concourse.bass as bass
from concourse import mybir

F32 = mybir.dt.float32
F32R = mybir.dt.float32r
ACT = mybir.ActivationFunctionType
ALU = mybir.AluOpType
AX_X = mybir.AxisListType.X

MASKED = -9000000000000000.0
EPS = 1e-5


def graph_attention(nc, xT, x, adj, wq, wk, wv, bq, bk, bv, beta, identity, out):
    B, N, D = x.shape
    P = 128
    H = 12
    HD = D // H
    C = D // P
    J = H // C
    PAIRS = B // 2
    W2 = 2 * N
    SCALE = float(HD) ** -0.5
    LOOPED = (1, PAIRS // 2 - 1)

    with ExitStack() as ctx:
        def sb(name, shape, dt=F32):
            return ctx.enter_context(nc.sbuf_tensor(name, shape, dt))

        def sem(name):
            return ctx.enter_context(nc.semaphore(name))

        w_raw = sb("w_raw", [P, 3, C, D])
        w_hi = sb("w_hi", [P, 3, C, D], F32R)
        w_lo = sb("w_lo", [P, 3, C, D], F32R)
        ident = sb("ident", [P, P])
        bq_col = sb("bq_col", [P, C])
        bqs_col = sb("bqs_col", [P, C])
        bk_col = sb("bk_col", [P, C])
        bv_row = sb("bv_row", [P, D])
        beta_col = sb("beta_col", [P, 1])
        power = sb("power", [P, 1])
        eps = sb("eps", [P, 1])
        warm = sb("warm", [P, 1])

        xT_raw = [sb(f"xT_raw{i}", [P, C, W2]) for i in range(2)]
        xT_hi = [sb(f"xT_hi{i}", [P, C, W2], F32R) for i in range(2)]
        xT_lo = [sb(f"xT_lo{i}", [P, C, W2], F32R) for i in range(2)]
        qT = [sb(f"qT{i}", [P, C, W2]) for i in range(2)]
        kT = [sb(f"kT{i}", [P, C, W2]) for i in range(2)]
        v = [sb(f"v{i}", [P, 2, D]) for i in range(2)]
        adj_raw = [sb(f"adj_raw{i}", [P, 2, N]) for i in range(2)]
        mask_neg = sb("mask_neg", [P, 2, N])
        mask_pos = sb("mask_pos", [P, 2, N])
        mask = [sb(f"mask{i}", [P, 2, N]) for i in range(2)]
        logits = [sb(f"logits{i}", [P, J, C, N]) for i in range(2)]
        neg_max = [sb(f"neg_max{i}", [P, H]) for i in range(2)]
        probs = [sb(f"probs{i}", [P, J, C, N]) for i in range(2)]
        row_sum = [sb(f"row_sum{i}", [P, J, C]) for i in range(4)]
        probsT = [sb(f"probsT{i}", [P, J, C, N]) for i in range(2)]
        attT = [sb(f"attT{i}", [P, C, N]) for i in range(2)]
        inv_sum = sb("inv_sum", [P, J, C])
        attended = sb("attended", [P, D])
        x_nat = [sb(f"x_nat{i}", [P, 2, D]) for i in range(2)]
        x_bv = [sb(f"x_bv{i}", [P, 2, D]) for i in range(2)]
        y = [sb(f"y{i}", [P, D]) for i in range(2)]
        stats = sb("stats", [P, 6])
        mean_var = [sb(f"mean_var{i}", [P, 2]) for i in range(2)]
        var_eps = sb("var_eps", [P, 1])
        rstd = [sb(f"rstd{i}", [P, 1]) for i in range(2)]
        normed = [sb(f"normed{i}", [P, 2, D]) for i in range(2)]

        ps_score = ctx.enter_context(nc.psum_tensor("ps_score", [P, J, 512], F32))
        ps_proj = ctx.enter_context(nc.psum_tensor("ps_proj", [P, 2, 512], F32))
        ps_attT = ctx.enter_context(nc.psum_tensor("ps_attT", [P, 512], F32))
        ps_att = ctx.enter_context(nc.psum_tensor("ps_att", [P, 512], F32))

        w_loaded = sem("w_loaded")
        const_loaded = sem("const_loaded")
        xT_loaded = [sem(f"xT_loaded{i}") for i in range(2)]
        x_loaded = [sem(f"x_loaded{i}") for i in range(2)]
        adj_loaded = [sem(f"adj_loaded{i}") for i in range(2)]
        out_stored = [sem(f"out_stored{i}") for i in range(2)]
        w_hi_ready = sem("w_hi_ready")
        w_ready = sem("w_ready")
        bqs_ready = sem("bqs_ready")
        power_ready = sem("power_ready")
        xhi_ready = sem("xhi_ready")
        xT_ready = sem("xT_ready")
        mneg_ready = sem("mneg_ready")
        mask_ready = sem("mask_ready")
        xbv_ready = sem("xbv_ready")
        proj_done = sem("proj_done")
        qk_copied = sem("qk_copied")
        v_copied = sem("v_copied")
        scores_done = sem("scores_done")
        logits_ready = sem("logits_ready")
        max_ready = sem("max_ready")
        probs_ready = sem("probs_ready")
        turned_a = sem("turned_a")
        turned_b = sem("turned_b")
        probsT_a = sem("probsT_a")
        probsT_b = sem("probsT_b")
        attT_done = sem("attT_done")
        attT_copied = sem("attT_copied")
        att_done = sem("att_done")
        inv_ready = sem("inv_ready")
        att_scaled = sem("att_scaled")
        y_ready = sem("y_ready")
        stats_ready = sem("stats_ready")
        meanvar_ready = sem("meanvar_ready")
        var_ready = sem("var_ready")
        rstd_ready = sem("rstd_ready")
        normed_ready = sem("normed_ready")

        def graph_exists(p, s, back):
            return not isinstance(p, int) or 0 <= 2 * p + s - back < B

        def pair_exists(p):
            return not isinstance(p, int) or p < PAIRS

        block = ctx.enter_context(nc.Block())

        @block.sync
        def _(sp):
            def load_xT(p, par):
                sp.dma_start(xT_raw[par][:], xT[bass.ds(p, 1)].rearrange("a p c n -> p (a c) n"))\
                    .then_inc(xT_loaded[par], 16)

            def load_x(p, par):
                sp.dma_start(x_nat[par][:], x[bass.ds(2 * p, 2)].rearrange("b n d -> n b d"))\
                    .then_inc(x_loaded[par], 16)

            def load_adj(p, par):
                sp.dma_start(adj_raw[par][:], adj[bass.ds(2 * p, 2)].rearrange("b n m -> n b m"))\
                    .then_inc(adj_loaded[par], 16)

            def pair(p, par):
                if pair_exists(p):
                    if not isinstance(p, int) or p >= 2:
                        sp.wait_ge(xbv_ready, p - 1)
                    load_x(p, par)
                if pair_exists(p + 2):
                    sp.wait_ge(mask_ready, p + 1)
                    load_adj(p + 2, par)
                if pair_exists(p + 3):
                    sp.wait_ge(xT_ready, p + 2)
                    load_xT(p + 3, 1 - par)
                if graph_exists(p, 0, 4):
                    sp.wait_ge(normed_ready, 2 * p - 2)
                    sp.dma_start(out[bass.ds(2 * p - 4, 2)].rearrange("b n d -> n b d"), normed[par][:])\
                        .then_inc(out_stored[par], 16)

            sp.dma_start(w_raw[:, 0], wq.rearrange("(c p) n -> p c n", p=P)).then_inc(w_loaded, 16)
            load_xT(0, 0)
            sp.dma_start(w_raw[:, 1], wk.rearrange("(c p) n -> p c n", p=P)).then_inc(w_loaded, 16)
            sp.dma_start(w_raw[:, 2], wv.rearrange("(c p) n -> p c n", p=P)).then_inc(w_loaded, 16)
            load_xT(1, 1)
            load_adj(0, 0)
            load_adj(1, 1)
            sp.wait_ge(xT_ready, 1)
            load_xT(2, 0)
            pair(0, 0)
            pair(1, 1)
            with sp.Fori(LOOPED[0], LOOPED[1] - 1) as quad:
                pair(2 * quad, 0)
                pair(2 * quad + 1, 1)
            for p in range(PAIRS - 4, PAIRS + 2):
                pair(p, p % 2)
            for par in range(2):
                sp.wait_ge(out_stored[par], 16 * PAIRS // 2)

        @block.tensor
        def _(pe):
            def scores(p, par, s):
                pe.wait_ge(qk_copied, 6 * p + 6)
                if graph_exists(p, s, 2):
                    pe.wait_ge(probsT_a, 2 * p + s - 1)
                    pe.wait_ge(probsT_b, 2 * p + s - 1)
                elif graph_exists(p, s, 1):
                    pe.wait_ge(logits_ready, 2 * p + s)
                for c in range(C):
                    for j in range(J):
                        rows = slice(HD * j, HD * j + HD)
                        mm = pe.matmul(ps_score[:, j, c * N:(c + 1) * N], qT[par][rows, c, s * N:(s + 1) * N],
                                       kT[par][rows, c, s * N:(s + 1) * N], start=True, stop=True)
                mm.then_inc(scores_done, 1)

            def turn_back(p, par, s):
                pe.wait_ge(attT_copied, 2 * p + s - 1)
                if graph_exists(p, s, 3):
                    pe.wait_ge(att_scaled, 2 * p + s - 2)
                for c in range(C):
                    mm = pe.transpose(ps_att[:, c * P:(c + 1) * P], attT[s][:, c, :], ident[:])
                mm.then_inc(att_done, 1)

            def turn_probs(p, s):
                pe.wait_ge(probs_ready, 2 * p + s)
                if graph_exists(p, s, 0):
                    pe.wait_ge(logits_ready, 2 * p + s + 1)
                for j in range(J):
                    for c in range(C):
                        mm = pe.transpose(ps_score[:, j, c * N:(c + 1) * N], probs[1 - s][:, j, c, :], ident[:])
                    if j == J // 2 - 1:
                        mm.then_inc(turned_a, 1)
                mm.then_inc(turned_b, 1)

            def attend(p, par, s):
                pe.wait_ge(probsT_a, 2 * p + s)
                pe.wait_ge(probsT_b, 2 * p + s)
                if graph_exists(p, s, 2):
                    pe.wait_ge(attT_copied, 2 * p + s - 1)
                if s:
                    pe.wait_ge(v_copied, 2 * p + 2)
                v_of = v[par] if s else v[1 - par]
                for c in range(C):
                    for j in range(J):
                        h = J * c + j
                        mm = pe.matmul(ps_attT[HD * j:HD * j + HD, c * N:(c + 1) * N],
                                       v_of[:, 1 - s, h * HD:(h + 1) * HD], probsT[1 - s][:, j, c, :],
                                       start=True, stop=True)
                mm.then_inc(attT_done, 1)

            def project(p, par, u):
                if u == 0:
                    pe.wait_ge(xT_ready, p + 1)
                if isinstance(p, int) and p == 0:
                    pe.wait_ge(w_ready, u // 3 + 1)
                if u >= 2:
                    pe.wait_ge(qk_copied, 6 * p + u - 1)
                elif not isinstance(p, int) or p > 0:
                    pe.wait_ge(v_copied, 2 * p - 1 + u)
                passes = ((w_hi, xT_hi), (w_lo, xT_hi), (w_hi, xT_lo))
                n = 0
                for c in range(C):
                    for w_half, x_half in passes:
                        if u < 6:
                            m = u % C
                            mm = pe.matmul(ps_proj[:, u % 2, 0:W2], w_half[:, u // C, c, m * P:(m + 1) * P],
                                           x_half[par][:, c, :], start=(n == 0), stop=(n == 3 * C - 1))
                        else:
                            mm = pe.matmul(ps_proj[:, u % 2, 0:D], x_half[par][:, c, (u - 6) * N:(u - 5) * N],
                                           w_half[:, 2, c, :], start=(n == 0), stop=(n == 3 * C - 1))
                        n += 1
                mm.then_inc(proj_done, 1)

            def slot(p, par, s):
                if graph_exists(p, s, 0):
                    scores(p, par, s)
                if graph_exists(p, s, 2):
                    turn_back(p, par, s)
                for half in range(2):
                    if pair_exists(p + 1):
                        project(p + 1, 1 - par, 4 * s + 2 * half)
                        project(p + 1, 1 - par, 4 * s + 2 * half + 1)
                    if graph_exists(p, s, 1):
                        if half == 0:
                            turn_probs(p, s)
                        else:
                            attend(p, par, s)

            for u in range(8):
                project(0, 0, u)
            pe.wait_ge(const_loaded, 16 * 5)
            for p in range(2):
                for s in range(2):
                    slot(p, p % 2, s)
            with pe.Fori(*LOOPED) as quad:
                for par in range(2):
                    for s in range(2):
                        slot(2 * quad + par, par, s)
            for p in range(PAIRS - 2, PAIRS + 1):
                for s in range(2):
                    slot(p, p % 2, s)

        @block.scalar
        def _(act):
            def exps(p, par, s, back, first, last):
                t = (s + back) % 2
                if first == 0:
                    act.wait_ge(max_ready, 2 * p + s - back + 1)
                    if graph_exists(p, s, back + 2):
                        act.wait_ge(turned_b, 2 * p + s - back - 1)
                for i in range(first, last):
                    j, c = i // C, i % C
                    e = act.activation(probs[t][:, j, c, :], logits[t][:, j, c, :], ACT.Exp,
                                       bias=neg_max[t][:, i:i + 1],
                                       accum_out=row_sum[(2 * par + s - back) % 4][:, j, c:c + 1])
                if last == H:
                    e.then_inc(probs_ready, 1)

            def copy_qk(p, par, u):
                act.wait_ge(proj_done, 8 * p + u + 1)
                if u == 0 and (not isinstance(p, int) or p >= 2):
                    act.wait_ge(scores_done, 2 * p - 2)
                dst, bias, scale = (qT, bqs_col, SCALE) if u < C else (kT, bk_col, 1.0)
                act.activation(dst[par][:, u % C, :], ps_proj[:, u % 2, 0:W2], ACT.Identity,
                               bias=bias[:, u % C:u % C + 1], scale=scale).then_inc(qk_copied, 1)

            def copy_probsT(p, s):
                act.wait_ge(turned_a, 2 * p + s)
                if graph_exists(p, s, 3):
                    act.wait_ge(attT_done, 2 * p + s - 2)
                act.copy(probsT[1 - s][:, 0:J // 2].rearrange("p j c n -> p j (c n)"),
                         ps_score[:, 0:J // 2, 0:D]).then_inc(probsT_a, 1)

            def slot(p, par, s):
                units = range(4 * s, min(4 * s + 4, 6)) if pair_exists(p + 1) else ()
                if graph_exists(p, s, 1):
                    exps(p, par, s, 1, 8, H)
                for u in units[0:2]:
                    copy_qk(p + 1, 1 - par, u)
                if graph_exists(p, s, 1):
                    copy_probsT(p, s)
                if graph_exists(p, s, 0):
                    exps(p, par, s, 0, 0, 4)
                for u in units[2:3]:
                    copy_qk(p + 1, 1 - par, u)
                if graph_exists(p, s, 0):
                    exps(p, par, s, 0, 4, 6)
                for u in units[3:4]:
                    copy_qk(p + 1, 1 - par, u)
                if graph_exists(p, s, 0):
                    exps(p, par, s, 0, 6, 8)

            act.wait_ge(const_loaded, 16 * 5)
            act.mul(bqs_col[:], bq_col[:], SCALE).then_inc(bqs_ready, 1)
            act.wait_ge(bqs_ready, 1)
            act.activation(warm[:], bqs_col[:, 0:1], ACT.Exp)
            for u in range(6):
                copy_qk(0, 0, u)
            for p in range(2):
                for s in range(2):
                    slot(p, p % 2, s)
            with act.Fori(*LOOPED) as quad:
                for par in range(2):
                    for s in range(2):
                        slot(2 * quad + par, par, s)
            for p in range(PAIRS - 2, PAIRS + 1):
                for s in range(2):
                    slot(p, p % 2, s)

        @block.vector
        def _(dve):
            def count(p, n):
                return n * p

            def split_w(i):
                dve.wait_ge(w_loaded, 16 * 3)
                dve.tensor_copy(w_hi[:, i], w_raw[:, i]).then_inc(w_hi_ready, 1)
                dve.wait_ge(w_hi_ready, i + 1)
                dve.tensor_tensor(w_lo[:, i], w_raw[:, i], w_hi[:, i], ALU.subtract).then_inc(w_ready, 1)

            def split_x(p, par, n):
                dve.wait_ge(xT_loaded[par], 16 * n)
                if not isinstance(p, int) or p >= 2:
                    dve.wait_ge(proj_done, 8 * p - 8)
                dve.tensor_copy(xT_hi[par][:], xT_raw[par][:]).then_inc(xhi_ready, 1)
                dve.wait_ge(xhi_ready, p + 1)
                dve.tensor_tensor(xT_lo[par][:], xT_raw[par][:], xT_hi[par][:], ALU.subtract)\
                    .then_inc(xT_ready, 1)

            def make_mask(p, par, n):
                dve.wait_ge(adj_loaded[par], 16 * n)
                dve.tensor_scalar(mask_neg[:], adj_raw[par][:], 0.0, MASKED, ALU.is_le, ALU.mult)
                dve.tensor_scalar(mask_pos[:], adj_raw[par][:], 0.0, beta_col[:], ALU.max, ALU.mult)\
                    .then_inc(mneg_ready, 1)
                dve.wait_ge(mneg_ready, p + 1)
                dve.tensor_tensor(mask[par][:], mask_neg[:], mask_pos[:], ALU.add).then_inc(mask_ready, 1)

            def make_logits(p, par, s):
                b = 2 * p + s
                dve.wait_ge(scores_done, b + 1)
                if s == 0:
                    dve.wait_ge(mask_ready, p + 1)
                if graph_exists(p, s, 2):
                    dve.wait_ge(probs_ready, b - 1)
                of_graph = mask[par][:, s, :].unsqueeze(1).unsqueeze(1).broadcast_to([P, J, C, N])
                if graph_exists(p, s, 3):
                    dve.wait_ge(stats_ready, b - 2)
                dve.tensor_tensor(logits[s][:], ps_score[:, :, 0:D].rearrange("p j (c n) -> p j c n", c=C),
                                  of_graph, ALU.add).then_inc(logits_ready, 1)
                if graph_exists(p, s, 3):
                    dve.bn_aggr(mean_var[1 - s][:], stats[:]).then_inc(meanvar_ready, 1)
                dve.wait_ge(logits_ready, b + 1)
                dve.tensor_reduce(neg_max[s][:], logits[s][:].rearrange("p j c n -> p (j c) n"), AX_X, ALU.max,
                                  negate=True).then_inc(max_ready, 1)

            def copy_probsT(p, s):
                dve.wait_ge(turned_b, 2 * p + s)
                if graph_exists(p, s, 3):
                    dve.wait_ge(attT_done, 2 * p + s - 2)
                dve.tensor_copy(probsT[1 - s][:, J // 2:J].rearrange("p j c n -> p j (c n)"),
                                ps_score[:, J // 2:J, 0:D]).then_inc(probsT_b, 1)

            def copy_v(p, par, g):
                dve.wait_ge(proj_done, 8 * p + 7 + g)
                if not isinstance(p, int) or p >= 2:
                    dve.wait_ge(attT_done, 2 * p - 2)
                dve.tensor_copy(v[par][:, g, :], ps_proj[:, g, 0:D]).then_inc(v_copied, 1)

            def copy_attT(p, s):
                dve.wait_ge(attT_done, 2 * p + s)
                if graph_exists(p, s, 3):
                    dve.wait_ge(att_done, 2 * p + s - 2)
                dve.tensor_copy(attT[1 - s][:].rearrange("p c n -> p (c n)"), ps_attT[:, 0:D])\
                    .then_inc(attT_copied, 1)

            def residual(p, par, s):
                n = 2 * p + s - 2
                t = 1 - s
                dve.wait_ge(probs_ready, n)
                dve.reciprocal(inv_sum[:], row_sum[(2 * par + s - 3) % 4][:]).then_inc(inv_ready, 1)
                dve.wait_ge(inv_ready, n)
                dve.wait_ge(att_done, n)
                dve.tensor_tensor(attended[:].rearrange("p (c j d) -> p c j d", c=C, j=J),
                                  ps_att[:, 0:D].rearrange("p (c j d) -> p c j d", c=C, j=J),
                                  inv_sum[:].rearrange("p j c -> p c j").unsqueeze(3).broadcast_to([P, C, J, HD]),
                                  ALU.mult).then_inc(att_scaled, 1)
                dve.wait_ge(att_scaled, n)
                dve.wait_ge(xbv_ready, p if s else p - 1)
                if graph_exists(p, s, 5):
                    dve.wait_ge(normed_ready, n - 2)
                x_of = x_bv[1 - par] if s else x_bv[par]
                dve.tensor_tensor(y[t][:], attended[:], x_of[:, 1 - s, :], ALU.add).then_inc(y_ready, 1)
                dve.wait_ge(y_ready, n)
                dve.bn_stats(stats[:], y[t][:]).then_inc(stats_ready, 1)

            def normalize(p, par, s, stored):
                n = 2 * p + s - 3
                dve.wait_ge(rstd_ready, n)
                if s == 0 and stored is not None:
                    dve.wait_ge(out_stored[par], 16 * stored)
                dve.tensor_scalar(normed[par][:, s, :], y[s][:], mean_var[s][:, 0:1], rstd[s][:, 0:1],
                                  ALU.subtract, ALU.mult).then_inc(normed_ready, 1)

            def slot(p, par, s, quad):
                if graph_exists(p, s, 4):
                    stored = quad - 1 if not isinstance(p, int) or p >= 4 else None
                    normalize(p, par, s, stored)
                if graph_exists(p, s, 3):
                    residual(p, par, s)
                if graph_exists(p, s, 0):
                    make_logits(p, par, s)
                elif graph_exists(p, s, 3):
                    dve.wait_ge(stats_ready, 2 * p + s - 2)
                    dve.bn_aggr(mean_var[1 - s][:], stats[:]).then_inc(meanvar_ready, 1)
                if graph_exists(p, s, 1):
                    copy_probsT(p, s)
                if s == 0:
                    if pair_exists(p + 2):
                        split_x(p + 2, par, quad + 2)
                else:
                    if pair_exists(p + 1):
                        copy_v(p + 1, 1 - par, 0)
                        make_mask(p + 1, 1 - par, quad + 1 + par)
                        copy_v(p + 1, 1 - par, 1)
                if graph_exists(p, s, 1):
                    copy_attT(p, s)

            split_w(0)
            split_x(0, 0, 1)
            split_w(1)
            split_w(2)
            split_x(1, 1, 1)
            dve.wait_ge(const_loaded, 16 * 5)
            make_mask(0, 0, 1)
            copy_v(0, 0, 0)
            copy_v(0, 0, 1)
            for p in range(2):
                for s in range(2):
                    slot(p, p % 2, s, p // 2)
            with dve.Fori(*LOOPED) as quad:
                for par in range(2):
                    for s in range(2):
                        slot(2 * quad + par, par, s, quad)
            for p in range(PAIRS - 2, PAIRS + 2):
                for s in range(2):
                    slot(p, p % 2, s, p // 2)

        @block.gpsimd
        def _(pool):
            def add_bv(p, par, n):
                pool.wait_ge(x_loaded[par], 16 * n)
                if not isinstance(p, int) or p >= 2:
                    pool.wait_ge(y_ready, 2 * p - 2)
                pool.tensor_tensor(x_bv[par][:], x_nat[par][:], bv_row[:].unsqueeze(1).broadcast_to([P, 2, D]),
                                   ALU.add).then_inc(xbv_ready, 1)

            def make_rstd(p, s):
                n = 2 * p + s - 2
                t = 1 - s
                pool.wait_ge(meanvar_ready, n)
                pool.tensor_tensor(var_eps[:], mean_var[t][:, 1:2], eps[:], ALU.add).then_inc(var_ready, 1)
                pool.wait_ge(var_ready, n)
                if graph_exists(p, s, 5):
                    pool.wait_ge(normed_ready, n - 2)
                pool.tensor_tensor(rstd[t][:], var_eps[:], power[:], ALU.pow).then_inc(rstd_ready, 1)

            def slot(p, par, s, quad):
                if s == 0 and pair_exists(p - 1) and (not isinstance(p, int) or p >= 1):
                    add_bv(p - 1, 1 - par, quad + par)
                if graph_exists(p, s, 3):
                    make_rstd(p, s)

            pool.memset(eps[:], EPS)
            pool.memset(power[:], -0.5).then_inc(power_ready, 1)
            pool.dma_start(ident[:], identity).then_inc(const_loaded, 16)
            pool.dma_start(bq_col[:], bq).then_inc(const_loaded, 16)
            pool.dma_start(bk_col[:], bk).then_inc(const_loaded, 16)
            pool.dma_start(bv_row[:], bv.to_broadcast([P, D])).then_inc(const_loaded, 16)
            pool.dma_start(beta_col[:], beta.to_broadcast([P, 1])).then_inc(const_loaded, 16)
            pool.wait_ge(power_ready, 1)
            pool.wait_ge(const_loaded, 16 * 5)
            for p in range(2):
                for s in range(2):
                    slot(p, p % 2, s, p // 2)
            with pool.Fori(*LOOPED) as quad:
                for par in range(2):
                    for s in range(2):
                        slot(2 * quad + par, par, s, quad)
            for p in range(PAIRS - 2, PAIRS + 2):
                for s in range(2):
                    slot(p, p % 2, s, p // 2)


def kernel(x, adj, L0_gnn_Wq, L0_gnn_bq, L0_gnn_Wk, L0_gnn_bk, L0_gnn_Wv, L0_gnn_bv, L0_gnn_beta):
    import numpy as np
    import concourse.bacc as bacc
    from concourse.bass_utils import run_bass_kernel_spmd

    B, N, D = x.shape
    C = D // 128
    x = np.ascontiguousarray(x)
    arrays = {
        "xT": np.ascontiguousarray(x.reshape(B // 2, 2, N, C, 128).transpose(0, 4, 3, 1, 2)
                                   .reshape(B // 2, 128, C, 2 * N)),
        "x": x,
        "adj": np.ascontiguousarray(adj),
        "wq": np.ascontiguousarray(L0_gnn_Wq),
        "wk": np.ascontiguousarray(L0_gnn_Wk),
        "wv": np.ascontiguousarray(L0_gnn_Wv),
        "bq": np.ascontiguousarray(np.asarray(L0_gnn_bq).reshape(C, 128).T),
        "bk": np.ascontiguousarray(np.asarray(L0_gnn_bk).reshape(C, 128).T),
        "bv": np.ascontiguousarray(np.asarray(L0_gnn_bv).reshape(1, D)),
        "beta": np.ascontiguousarray(np.asarray(L0_gnn_beta).reshape(1, 1)),
        "identity": np.eye(128, dtype=np.float32),
    }
    nc = bacc.Bacc("TRN2", target_bir_lowering=False, num_devices=1)
    args = [nc.dram_tensor(f"in_{n}", a.shape, mybir.dt.from_np(a.dtype), kind="ExternalInput").ap()
            for n, a in arrays.items()]
    out = nc.dram_tensor("out", (B, N, D), mybir.dt.float32, kind="ExternalOutput").ap()
    graph_attention(nc, *args, out)
    r = run_bass_kernel_spmd(nc, [{f"in_{n}": a for n, a in arrays.items()}], core_ids=[0])
    return r.results[0]["out"]
```

```python
from contextlib import ExitStack

import concourse.bass as bass
from concourse import mybir

F32 = mybir.dt.float32
F32R = mybir.dt.float32r
ACT = mybir.ActivationFunctionType
ALU = mybir.AluOpType
AX_X = mybir.AxisListType.X

MASKED = -9000000000000000.0
EPS = 1e-5


def graph_attention(nc, xT, x, adj, wq, wk, wv, bq, bk, bv, beta, identity, out):
    B, N, D = x.shape
    P = 128
    H = 12
    HD = D // H
    C = D // P
    J = H // C
    PAIRS = B // 2
    W2 = 2 * N
    SCALE = float(HD) ** -0.5
    LOOPED = (1, PAIRS // 2 - 1)

    with ExitStack() as ctx:
        def sb(name, shape, dt=F32):
            return ctx.enter_context(nc.sbuf_tensor(name, shape, dt))

        def sem(name):
            return ctx.enter_context(nc.semaphore(name))

        w_raw = sb("w_raw", [P, 3, C, D])
        w_hi = sb("w_hi", [P, 3, C, D], F32R)
        w_lo = sb("w_lo", [P, 3, C, D], F32R)
        ident = sb("ident", [P, P])
        bq_col = sb("bq_col", [P, C])
        bqs_col = sb("bqs_col", [P, C])
        bk_col = sb("bk_col", [P, C])
        bv_row = sb("bv_row", [P, D])
        beta_col = sb("beta_col", [P, 1])
        power = sb("power", [P, 1])
        eps = sb("eps", [P, 1])
        warm = sb("warm", [P, 1])

        xT_raw = [sb(f"xT_raw{i}", [P, C, W2]) for i in range(2)]
        xT_hi = [sb(f"xT_hi{i}", [P, C, W2], F32R) for i in range(2)]
        xT_lo = [sb(f"xT_lo{i}", [P, C, W2], F32R) for i in range(2)]
        qT = [sb(f"qT{i}", [P, C, W2]) for i in range(2)]
        kT = [sb(f"kT{i}", [P, C, W2]) for i in range(2)]
        v = [sb(f"v{i}", [P, 2, D]) for i in range(2)]
        adj_raw = [sb(f"adj_raw{i}", [P, 2, N]) for i in range(2)]
        mask_neg = sb("mask_neg", [P, 2, N])
        mask_pos = sb("mask_pos", [P, 2, N])
        mask = [sb(f"mask{i}", [P, 2, N]) for i in range(2)]
        logits = [sb(f"logits{i}", [P, J, C, N]) for i in range(2)]
        neg_max = [sb(f"neg_max{i}", [P, H]) for i in range(2)]
        probs = [sb(f"probs{i}", [P, J, C, N]) for i in range(2)]
        row_sum = [sb(f"row_sum{i}", [P, J, C]) for i in range(4)]
        probsT = [sb(f"probsT{i}", [P, J, C, N]) for i in range(2)]
        attT = [sb(f"attT{i}", [P, C, N]) for i in range(2)]
        inv_sum = sb("inv_sum", [P, J, C])
        attended = sb("attended", [P, D])
        x_nat = [sb(f"x_nat{i}", [P, 2, D]) for i in range(2)]
        x_bv = [sb(f"x_bv{i}", [P, 2, D]) for i in range(2)]
        y = [sb(f"y{i}", [P, D]) for i in range(2)]
        stats = sb("stats", [P, 6])
        mean_var = [sb(f"mean_var{i}", [P, 2]) for i in range(2)]
        var_eps = sb("var_eps", [P, 1])
        rstd = [sb(f"rstd{i}", [P, 1]) for i in range(2)]
        normed = [sb(f"normed{i}", [P, 2, D]) for i in range(2)]

        ps_score = ctx.enter_context(nc.psum_tensor("ps_score", [P, J, 512], F32))
        ps_proj = ctx.enter_context(nc.psum_tensor("ps_proj", [P, 2, 512], F32))
        ps_attT = ctx.enter_context(nc.psum_tensor("ps_attT", [P, 512], F32))
        ps_att = ctx.enter_context(nc.psum_tensor("ps_att", [P, 512], F32))

        w_loaded = [[sem(f"w_loaded_{n}{c}") for c in range(C)] for n in "qkv"]
        const_loaded = sem("const_loaded")
        ident_loaded = sem("ident_loaded")
        bv_loaded = sem("bv_loaded")
        xT_loaded = [sem(f"xT_loaded{i}") for i in range(2)]
        x_loaded = [sem(f"x_loaded{i}") for i in range(2)]
        adj_loaded = [sem(f"adj_loaded{i}") for i in range(2)]
        out_stored = [sem(f"out_stored{i}") for i in range(2)]
        w_hi_ready = sem("w_hi_ready")
        w_ready = sem("w_ready")
        bqs_ready = sem("bqs_ready")
        power_ready = sem("power_ready")
        xhi_ready = sem("xhi_ready")
        xT_ready = sem("xT_ready")
        mneg_ready = sem("mneg_ready")
        mask_ready = sem("mask_ready")
        xbv_ready = sem("xbv_ready")
        proj_done = sem("proj_done")
        qk_copied = sem("qk_copied")
        v_copied = sem("v_copied")
        max_ready = sem("max_ready")
        probs_ready = sem("probs_ready")
        scores_done = sem("scores_done")
        logits_ready = sem("logits_ready")
        turned_a = sem("turned_a")
        turned_b = sem("turned_b")
        probsT_a = sem("probsT_a")
        probsT_b = sem("probsT_b")
        attT_done = sem("attT_done")
        attT_copied = sem("attT_copied")
        att_done = sem("att_done")
        inv_ready = sem("inv_ready")
        att_scaled = sem("att_scaled")
        y_ready = sem("y_ready")
        stats_ready = sem("stats_ready")
        meanvar_ready = sem("meanvar_ready")
        var_ready = sem("var_ready")
        rstd_ready = sem("rstd_ready")
        normed_ready = sem("normed_ready")

        def graph_exists(p, s, back):
            return not isinstance(p, int) or 0 <= 2 * p + s - back < B

        def pair_exists(p):
            return not isinstance(p, int) or p < PAIRS

        block = ctx.enter_context(nc.Block())

        @block.sync
        def _(sp):
            def load_xT(p, par):
                sp.dma_start(xT_raw[par][:], xT[bass.ds(p, 1)].rearrange("a p c n -> p (a c) n"))\
                    .then_inc(xT_loaded[par], 16)

            def load_x(p, par):
                sp.dma_start(x_nat[par][:], x[bass.ds(2 * p, 2)].rearrange("b n d -> n b d"))\
                    .then_inc(x_loaded[par], 16)

            def load_adj(p, par):
                sp.dma_start(adj_raw[par][:], adj[bass.ds(2 * p, 2)].rearrange("b n m -> n b m"))\
                    .then_inc(adj_loaded[par], 16)

            def pair(p, par):
                if pair_exists(p):
                    if not isinstance(p, int) or p >= 2:
                        sp.wait_ge(xbv_ready, p - 1)
                    load_x(p, par)
                if pair_exists(p + 2):
                    sp.wait_ge(mask_ready, p + 1)
                    load_adj(p + 2, par)
                if pair_exists(p + 3):
                    sp.wait_ge(xT_ready, p + 2)
                    load_xT(p + 3, 1 - par)
                if graph_exists(p, 0, 4):
                    sp.wait_ge(normed_ready, 2 * p - 2)
                    sp.dma_start(out[bass.ds(2 * p - 4, 2)].rearrange("b n d -> n b d"), normed[par][:])\
                        .then_inc(out_stored[par], 16)

            load_xT(0, 0)
            for i, w in enumerate((wq, wk, wv)):
                for c in range(C):
                    sp.dma_start(w_raw[:, i, c], w[c * P:(c + 1) * P, :]).then_inc(w_loaded[i][c], 16)
            sp.dma_start(ident[:], identity).then_inc(ident_loaded, 16)
            sp.dma_start(bv_row[:], bv.to_broadcast([P, D])).then_inc(bv_loaded, 16)
            load_xT(1, 1)
            load_adj(0, 0)
            load_adj(1, 1)
            sp.wait_ge(xT_ready, 1)
            load_xT(2, 0)
            pair(0, 0)
            pair(1, 1)
            with sp.Fori(LOOPED[0], LOOPED[1] - 1) as quad:
                pair(2 * quad, 0)
                pair(2 * quad + 1, 1)
            for p in range(PAIRS - 4, PAIRS + 2):
                pair(p, p % 2)
            for par in range(2):
                sp.wait_ge(out_stored[par], 16 * PAIRS // 2)

        @block.tensor
        def _(pe):
            def scores(p, par, s, chunks):
                if chunks[0] == 0:
                    if graph_exists(p, s, 2):
                        pe.wait_ge(probsT_a, 2 * p + s - 1)
                        pe.wait_ge(probsT_b, 2 * p + s - 1)
                    elif graph_exists(p, s, 1):
                        pe.wait_ge(logits_ready, 2 * p + s)
                for c in chunks:
                    if s == 0:
                        pe.wait_ge(qk_copied, 6 * p + 4 + c)
                    for j in range(J):
                        rows = slice(HD * j, HD * j + HD)
                        mm = pe.matmul(ps_score[:, j, c * N:(c + 1) * N], qT[par][rows, c, s * N:(s + 1) * N],
                                       kT[par][rows, c, s * N:(s + 1) * N], start=True, stop=True)
                if chunks[-1] == C - 1:
                    mm.then_inc(scores_done, 1)

            def turn_back(p, par, s):
                pe.wait_ge(attT_copied, 2 * p + s - 1)
                if graph_exists(p, s, 3):
                    pe.wait_ge(att_scaled, 2 * p + s - 2)
                for c in range(C):
                    mm = pe.transpose(ps_att[:, c * P:(c + 1) * P], attT[s][:, c, :], ident[:])
                mm.then_inc(att_done, 1)

            def turn_probs(p, s):
                if graph_exists(p, s, 0):
                    pe.wait_ge(logits_ready, 2 * p + s + 1)
                for j in range(J):
                    if j % (J // 2) == 0:
                        pe.wait_ge(probs_ready, 4 * p + 2 * s - 1 + j // (J // 2))
                    for c in range(C):
                        mm = pe.transpose(ps_score[:, j, c * N:(c + 1) * N], probs[1 - s][:, j, c, :], ident[:])
                    if j == J // 2 - 1:
                        mm.then_inc(turned_a, 1)
                mm.then_inc(turned_b, 1)

            def attend(p, par, s):
                pe.wait_ge(probsT_a, 2 * p + s)
                if graph_exists(p, s, 2):
                    pe.wait_ge(attT_copied, 2 * p + s - 1)
                if s:
                    pe.wait_ge(v_copied, 2 * p + 2)
                v_of = v[par] if s else v[1 - par]
                for half in range(2):
                    if half == 1:
                        pe.wait_ge(probsT_b, 2 * p + s)
                    for c, j in ((c, half * J // 2 + j) for c in range(C) for j in range(J // 2)):
                        h = J * c + j
                        mm = pe.matmul(ps_attT[HD * j:HD * j + HD, c * N:(c + 1) * N],
                                       v_of[:, 1 - s, h * HD:(h + 1) * HD], probsT[1 - s][:, j, c, :],
                                       start=True, stop=True)
                mm.then_inc(attT_done, 1)

            def project(p, par, u):
                if u == 0:
                    pe.wait_ge(xT_ready, p + 1)
                if u >= 2:
                    pe.wait_ge(qk_copied, 6 * p + u - 1)
                elif not isinstance(p, int) or p > 0:
                    pe.wait_ge(v_copied, 2 * p - 1 + u)
                passes = ((w_hi, xT_hi), (w_lo, xT_hi), (w_hi, xT_lo))
                n = 0
                for c in range(C):
                    if isinstance(p, int) and p == 0:
                        pe.wait_ge(w_ready, C * (u // 3) + c + 1)
                    for w_half, x_half in passes:
                        if u < 6:
                            m = u % C
                            mm = pe.matmul(ps_proj[:, u % 2, 0:W2], w_half[:, u // C, c, m * P:(m + 1) * P],
                                           x_half[par][:, c, :], start=(n == 0), stop=(n == 3 * C - 1))
                        else:
                            mm = pe.matmul(ps_proj[:, u % 2, 0:D], x_half[par][:, c, (u - 6) * N:(u - 5) * N],
                                           w_half[:, 2, c, :], start=(n == 0), stop=(n == 3 * C - 1))
                        n += 1
                mm.then_inc(proj_done, 1)

            def unit(p, par, s, n):
                if s == 0 and n < 2:
                    if pair_exists(p):
                        project(p, par, 6 + n)
                elif pair_exists(p + 1):
                    project(p + 1, 1 - par, 4 * s + n - 2)

            def slot(p, par, s):
                if graph_exists(p, s, 0):
                    scores(p, par, s, (0,))
                unit(p, par, s, 0)
                if graph_exists(p, s, 0):
                    scores(p, par, s, (1, 2))
                if graph_exists(p, s, 2):
                    turn_back(p, par, s)
                unit(p, par, s, 1)
                unit(p, par, s, 2)
                if graph_exists(p, s, 1):
                    turn_probs(p, s)
                unit(p, par, s, 3)
                if graph_exists(p, s, 1):
                    attend(p, par, s)

            for u in range(6):
                project(0, 0, u)
            pe.wait_ge(ident_loaded, 16)
            for p in range(2):
                for s in range(2):
                    slot(p, p % 2, s)
            with pe.Fori(*LOOPED) as quad:
                for par in range(2):
                    for s in range(2):
                        slot(2 * quad + par, par, s)
            for p in range(PAIRS - 2, PAIRS + 1):
                for s in range(2):
                    slot(p, p % 2, s)

        @block.scalar
        def _(act):
            def exps(p, par, s, back, first, last):
                t = (s + back) % 2
                if first == 0:
                    act.wait_ge(max_ready, 4 * p + 2 * (s - back) + 1)
                    if graph_exists(p, s, back + 2):
                        act.wait_ge(turned_b, 2 * p + s - back - 1)
                for i in range(first, last):
                    if i == H // 2:
                        act.wait_ge(max_ready, 4 * p + 2 * (s - back) + 2)
                    j, c = i // C, i % C
                    e = act.activation(probs[t][:, j, c, :], logits[t][:, j, c, :], ACT.Exp,
                                       bias=neg_max[t][:, i:i + 1],
                                       accum_out=row_sum[(2 * par + s - back) % 4][:, j, c:c + 1])
                    if i in (H // 2 - 1, H - 1):
                        e.then_inc(probs_ready, 1)

            def copy_qk(p, par, u):
                act.wait_ge(proj_done, 8 * p + u + 1)
                if u == 0 and (not isinstance(p, int) or p >= 2):
                    act.wait_ge(scores_done, 2 * p - 2)
                dst, bias, scale = (qT, bqs_col, SCALE) if u < C else (kT, bk_col, 1.0)
                act.activation(dst[par][:, u % C, :], ps_proj[:, u % 2, 0:W2], ACT.Identity,
                               bias=bias[:, u % C:u % C + 1], scale=scale).then_inc(qk_copied, 1)

            def copy_probsT(p, s):
                act.wait_ge(turned_a, 2 * p + s)
                if graph_exists(p, s, 3):
                    act.wait_ge(attT_done, 2 * p + s - 2)
                act.copy(probsT[1 - s][:, 0:J // 2].rearrange("p j c n -> p j (c n)"),
                         ps_score[:, 0:J // 2, 0:D]).then_inc(probsT_a, 1)

            def copy_attT(p, s):
                act.wait_ge(attT_done, 2 * p + s)
                if graph_exists(p, s, 3):
                    act.wait_ge(att_done, 2 * p + s - 2)
                act.copy(attT[1 - s][:].rearrange("p c n -> p (c n)"), ps_attT[:, 0:D]).then_inc(attT_copied, 1)

            def slot(p, par, s):
                units = ((2, 3, 4, 5) if s else (None, None, 0, 1)) if pair_exists(p + 1) else (None,) * 4

                def copy_unit(n):
                    if units[n] is not None:
                        copy_qk(p + 1, 1 - par, units[n])

                if graph_exists(p, s, 1):
                    exps(p, par, s, 1, 5, 8)
                copy_unit(0)
                if graph_exists(p, s, 1):
                    exps(p, par, s, 1, 8, H)
                copy_unit(1)
                copy_unit(2)
                if graph_exists(p, s, 1):
                    copy_probsT(p, s)
                if graph_exists(p, s, 0):
                    exps(p, par, s, 0, 0, 2)
                copy_unit(3)
                if graph_exists(p, s, 0):
                    exps(p, par, s, 0, 2, 3)
                if graph_exists(p, s, 1):
                    copy_attT(p, s)
                if graph_exists(p, s, 0):
                    exps(p, par, s, 0, 3, 5)

            def round_w(i):
                for c in range(C):
                    act.wait_ge(w_loaded[i][c], 16)
                    act.copy(w_hi[:, i, c], w_raw[:, i, c]).then_inc(w_hi_ready, 1)

            round_w(0)
            act.wait_ge(const_loaded, 16 * 3)
            act.mul(bqs_col[:], bq_col[:], SCALE).then_inc(bqs_ready, 1)
            act.wait_ge(bqs_ready, 1)
            act.activation(warm[:], bqs_col[:, 0:1], ACT.Exp)
            round_w(1)
            for u in range(6):
                copy_qk(0, 0, u)
            round_w(2)
            for p in range(2):
                for s in range(2):
                    slot(p, p % 2, s)
            with act.Fori(*LOOPED) as quad:
                for par in range(2):
                    for s in range(2):
                        slot(2 * quad + par, par, s)
            for p in range(PAIRS - 2, PAIRS + 1):
                for s in range(2):
                    slot(p, p % 2, s)

        @block.vector
        def _(dve):
            def split_w(i):
                for c in range(C):
                    dve.wait_ge(w_hi_ready, C * i + c + 1)
                    dve.tensor_tensor(w_lo[:, i, c], w_raw[:, i, c], w_hi[:, i, c], ALU.subtract)\
                        .then_inc(w_ready, 1)

            def split_x(p, par, n):
                dve.wait_ge(xT_loaded[par], 16 * n)
                if not isinstance(p, int) or p >= 2:
                    dve.wait_ge(proj_done, 8 * p - 8)
                dve.tensor_copy(xT_hi[par][:], xT_raw[par][:]).then_inc(xhi_ready, 1)
                dve.wait_ge(xhi_ready, p + 1)
                dve.tensor_tensor(xT_lo[par][:], xT_raw[par][:], xT_hi[par][:], ALU.subtract)\
                    .then_inc(xT_ready, 1)

            def make_mask(p, par, n):
                dve.wait_ge(adj_loaded[par], 16 * n)
                dve.tensor_scalar(mask_neg[:], adj_raw[par][:], 0.0, MASKED, ALU.is_le, ALU.mult)
                dve.tensor_scalar(mask_pos[:], adj_raw[par][:], 0.0, beta_col[:], ALU.max, ALU.mult)\
                    .then_inc(mneg_ready, 1)
                dve.wait_ge(mneg_ready, p + 1)
                dve.tensor_tensor(mask[par][:], mask_neg[:], mask_pos[:], ALU.add).then_inc(mask_ready, 1)

            def make_logits(p, par, s):
                b = 2 * p + s
                dve.wait_ge(scores_done, b + 1)
                if s == 0:
                    dve.wait_ge(mask_ready, p + 1)
                if graph_exists(p, s, 2):
                    dve.wait_ge(probs_ready, 4 * p + 2 * s - 2)
                of_graph = mask[par][:, s, :].unsqueeze(1).unsqueeze(1).broadcast_to([P, J, C, N])
                dve.tensor_tensor(logits[s][:], ps_score[:, :, 0:D].rearrange("p j (c n) -> p j c n", c=C),
                                  of_graph, ALU.add).then_inc(logits_ready, 1)

            def make_max(p, s, half):
                dve.wait_ge(logits_ready, 2 * p + s + 1)
                rows = slice(half * J // 2, (half + 1) * J // 2)
                dve.tensor_reduce(neg_max[s][:, half * H // 2:(half + 1) * H // 2],
                                  logits[s][:, rows].rearrange("p j c n -> p (j c) n"), AX_X, ALU.max,
                                  negate=True).then_inc(max_ready, 1)

            def copy_probsT(p, s):
                dve.wait_ge(turned_b, 2 * p + s)
                if graph_exists(p, s, 3):
                    dve.wait_ge(attT_done, 2 * p + s - 2)
                dve.tensor_copy(probsT[1 - s][:, J // 2:J].rearrange("p j c n -> p j (c n)"),
                                ps_score[:, J // 2:J, 0:D]).then_inc(probsT_b, 1)

            def copy_v(p, par, g):
                dve.wait_ge(proj_done, 8 * p + 7 + g)
                if not isinstance(p, int) or p >= 2:
                    dve.wait_ge(attT_done, 2 * p - 2)
                dve.tensor_copy(v[par][:, g, :], ps_proj[:, g, 0:D]).then_inc(v_copied, 1)

            def scale_attended(p, par, s):
                n = 2 * p + s - 2
                dve.wait_ge(probs_ready, 4 * p + 2 * s - 4)
                dve.reciprocal(inv_sum[:], row_sum[(2 * par + s - 3) % 4][:]).then_inc(inv_ready, 1)
                dve.wait_ge(inv_ready, n)
                dve.wait_ge(att_done, n)
                if graph_exists(p, s, 4):
                    dve.wait_ge(y_ready, n - 1)
                dve.tensor_tensor(attended[:].rearrange("p (c j d) -> p c j d", c=C, j=J),
                                  ps_att[:, 0:D].rearrange("p (c j d) -> p c j d", c=C, j=J),
                                  inv_sum[:].rearrange("p j c -> p c j").unsqueeze(3).broadcast_to([P, C, J, HD]),
                                  ALU.mult).then_inc(att_scaled, 1)

            def statistics(p, s):
                dve.wait_ge(y_ready, 2 * p + s - 2)
                dve.bn_stats(stats[:], y[1 - s][:]).then_inc(stats_ready, 1)

            def normalize(p, par, s, stored):
                n = 2 * p + s - 3
                dve.wait_ge(rstd_ready, n)
                if s == 0 and stored is not None:
                    dve.wait_ge(out_stored[par], 16 * stored)
                dve.tensor_scalar(normed[par][:, s, :], y[s][:], mean_var[s][:, 0:1], rstd[s][:, 0:1],
                                  ALU.subtract, ALU.mult).then_inc(normed_ready, 1)

            def slot(p, par, s, quad):
                if graph_exists(p, s, 3):
                    scale_attended(p, par, s)
                if graph_exists(p, s, 4):
                    stored = quad - 1 if not isinstance(p, int) or p >= 4 else None
                    normalize(p, par, s, stored)
                if s == 0 and pair_exists(p):
                    copy_v(p, par, 0)
                if s == 1 and pair_exists(p + 2):
                    split_x(p + 2, par, quad + 2)
                if graph_exists(p, s, 0):
                    make_logits(p, par, s)
                if graph_exists(p, s, 3):
                    statistics(p, s)
                if s == 0 and pair_exists(p):
                    copy_v(p, par, 1)
                if graph_exists(p, s, 0):
                    make_max(p, s, 0)
                if graph_exists(p, s, 3):
                    dve.wait_ge(stats_ready, 2 * p + s - 2)
                if graph_exists(p, s, 0) and graph_exists(p, s, 1):
                    copy_probsT(p, s)
                if graph_exists(p, s, 3):
                    dve.bn_aggr(mean_var[1 - s][:], stats[:]).then_inc(meanvar_ready, 1)
                if not graph_exists(p, s, 0) and graph_exists(p, s, 1):
                    copy_probsT(p, s)
                if graph_exists(p, s, 0):
                    make_max(p, s, 1)
                if s == 0 and pair_exists(p + 1):
                    make_mask(p + 1, 1 - par, quad + 1 + par)

            split_x(0, 0, 1)
            split_w(0)
            split_w(1)
            dve.wait_ge(const_loaded, 16 * 3)
            make_mask(0, 0, 1)
            split_x(1, 1, 1)
            split_w(2)
            for p in range(2):
                for s in range(2):
                    slot(p, p % 2, s, p // 2)
            with dve.Fori(*LOOPED) as quad:
                for par in range(2):
                    for s in range(2):
                        slot(2 * quad + par, par, s, quad)
            for p in range(PAIRS - 2, PAIRS + 2):
                for s in range(2):
                    slot(p, p % 2, s, p // 2)

        @block.gpsimd
        def _(pool):
            def add_bv(p, par, n):
                pool.wait_ge(x_loaded[par], 16 * n)
                if not isinstance(p, int) or p >= 2:
                    pool.wait_ge(y_ready, 2 * p - 2)
                pool.tensor_tensor(x_bv[par][:], x_nat[par][:], bv_row[:].unsqueeze(1).broadcast_to([P, 2, D]),
                                   ALU.add).then_inc(xbv_ready, 1)

            def residual(p, par, s):
                n = 2 * p + s - 2
                pool.wait_ge(att_scaled, n)
                pool.wait_ge(xbv_ready, p if s else p - 1)
                if graph_exists(p, s, 5):
                    pool.wait_ge(normed_ready, n - 2)
                x_of = x_bv[1 - par] if s else x_bv[par]
                pool.tensor_tensor(y[1 - s][:], attended[:], x_of[:, 1 - s, :], ALU.add).then_inc(y_ready, 1)

            def make_rstd(p, s):
                n = 2 * p + s - 2
                t = 1 - s
                pool.wait_ge(meanvar_ready, n)
                pool.tensor_tensor(var_eps[:], mean_var[t][:, 1:2], eps[:], ALU.add).then_inc(var_ready, 1)
                pool.wait_ge(var_ready, n)
                if graph_exists(p, s, 5):
                    pool.wait_ge(normed_ready, n - 2)
                pool.tensor_tensor(rstd[t][:], var_eps[:], power[:], ALU.pow).then_inc(rstd_ready, 1)

            def slot(p, par, s, quad):
                if s == 0 and pair_exists(p - 1) and (not isinstance(p, int) or p >= 1):
                    add_bv(p - 1, 1 - par, quad + par)
                if graph_exists(p, s, 3):
                    residual(p, par, s)
                    make_rstd(p, s)

            pool.dma_start(bq_col[:], bq).then_inc(const_loaded, 16)
            pool.dma_start(bk_col[:], bk).then_inc(const_loaded, 16)
            pool.dma_start(beta_col[:], beta.to_broadcast([P, 1])).then_inc(const_loaded, 16)
            pool.memset(eps[:], EPS)
            pool.memset(power[:], -0.5).then_inc(power_ready, 1)
            pool.wait_ge(power_ready, 1)
            pool.wait_ge(bv_loaded, 16)
            for p in range(2):
                for s in range(2):
                    slot(p, p % 2, s, p // 2)
            with pool.Fori(*LOOPED) as quad:
                for par in range(2):
                    for s in range(2):
                        slot(2 * quad + par, par, s, quad)
            for p in range(PAIRS - 2, PAIRS + 2):
                for s in range(2):
                    slot(p, p % 2, s, p // 2)


def kernel(x, adj, L0_gnn_Wq, L0_gnn_bq, L0_gnn_Wk, L0_gnn_bk, L0_gnn_Wv, L0_gnn_bv, L0_gnn_beta):
    import numpy as np
    import concourse.bacc as bacc
    from concourse.bass_utils import run_bass_kernel_spmd

    B, N, D = x.shape
    C = D // 128
    x = np.ascontiguousarray(x)
    arrays = {
        "xT": np.ascontiguousarray(x.reshape(B // 2, 2, N, C, 128).transpose(0, 4, 3, 1, 2)
                                   .reshape(B // 2, 128, C, 2 * N)),
        "x": x,
        "adj": np.ascontiguousarray(adj),
        "wq": np.ascontiguousarray(L0_gnn_Wq),
        "wk": np.ascontiguousarray(L0_gnn_Wk),
        "wv": np.ascontiguousarray(L0_gnn_Wv),
        "bq": np.ascontiguousarray(np.asarray(L0_gnn_bq).reshape(C, 128).T),
        "bk": np.ascontiguousarray(np.asarray(L0_gnn_bk).reshape(C, 128).T),
        "bv": np.ascontiguousarray(np.asarray(L0_gnn_bv).reshape(1, D)),
        "beta": np.ascontiguousarray(np.asarray(L0_gnn_beta).reshape(1, 1)),
        "identity": np.eye(128, dtype=np.float32),
    }
    nc = bacc.Bacc("TRN2", target_bir_lowering=False, num_devices=1)
    args = [nc.dram_tensor(f"in_{n}", a.shape, mybir.dt.from_np(a.dtype), kind="ExternalInput").ap()
            for n, a in arrays.items()]
    out = nc.dram_tensor("out", (B, N, D), mybir.dt.float32, kind="ExternalOutput").ap()
    graph_attention(nc, *args, out)
    r = run_bass_kernel_spmd(nc, [{f"in_{n}": a for n, a in arrays.items()}], core_ids=[0])
    return r.results[0]["out"]
```
